# Optimizing a Trainium2 kernel written in Bass

```python
import numpy as np
import jax
import jax.numpy as jnp

def _softmax(x, axis=-1):
    return jax.nn.softmax(x, axis=axis)

def _gelu(x):
    return jax.nn.gelu(x, approximate=True)

def _silu(x):
    return jax.nn.silu(x)

def _sigmoid(x):
    return jax.nn.sigmoid(x)

def _layernorm(x, axis=-1, eps=1e-05):
    m = jnp.mean(x, axis=axis, keepdims=True)
    v = jnp.var(x, axis=axis, keepdims=True)
    return (x - m) / jnp.sqrt(v + eps)

def _scatter_add(tgt, idx, src, axis=0):
    return tgt.at[idx].add(src)

def _segment_sum(src, seg, n):
    return jax.ops.segment_sum(src, seg, n)
kernel_name = 'mk_adj_seq_d2_adj_r2_1bf499'

def setup_inputs(seed: int=0):
    np.random.seed(seed)
    _w = jnp.asarray

    def _rec_inputs():
        import jax
        import jax.numpy as jnp
        _gk = jax.random.key(seed)
        x = 7.22e-05 + 1 * jax.random.normal(jax.random.fold_in(_gk, 1), (32, 256, 256), jnp.float32)
        _a = jax.random.bernoulli(jax.random.fold_in(_gk, 2), 0.03125, (32, 256, 256))
        adj = _a.astype(jnp.int32)
        return (x, adj)
    x, adj = _rec_inputs()

    def _L0_gnn_setup():
        import jax, jax.numpy as jnp
        import numpy as np
        import math
        D = 256
        B, L = (8, 1024)
        EPS = 1e-05

        def layer_norm(y, gamma, beta):
            mu = jnp.mean(y, axis=-1, keepdims=True)
            var = jnp.mean(jnp.square(y - mu), axis=-1, keepdims=True)
            return (y - mu) * jax.lax.rsqrt(var + EPS) * gamma + beta
        key = jax.random.key(seed)
        ks = jax.random.split(key, 8)
        s = 1.0 / math.sqrt(D)
        x = jax.random.normal(ks[0], (B, L, D), dtype=jnp.float32)
        adj = jax.random.randint(ks[1], (B, L, L), 0, 2, dtype=jnp.int32)
        Wq = jax.random.normal(ks[2], (D, D), dtype=jnp.float32) * s
        Wk = jax.random.normal(ks[3], (D, D), dtype=jnp.float32) * s
        Wv = jax.random.normal(ks[4], (D, D), dtype=jnp.float32) * s
        Wo = jax.random.normal(ks[5], (D, D), dtype=jnp.float32) * s
        bo = jnp.zeros((D,), dtype=jnp.float32)
        gamma = jnp.ones((D,), dtype=jnp.float32)
        beta = jnp.zeros((D,), dtype=jnp.float32)
        return {'x': x, 'adj': adj, 'Wq': Wq, 'Wk': Wk, 'Wv': Wv, 'Wo': Wo, 'bo': bo, 'gamma': gamma, 'beta': beta}
    _L0_gnn_all = _L0_gnn_setup()
    _L0_gnn_in = {k: v for k, v in _L0_gnn_all.items() if k in ('Wq', 'Wk', 'Wv', 'Wo', 'bo', 'gamma', 'beta')}
    del _L0_gnn_all

    def _L1_gnn_setup():
        import jax, jax.numpy as jnp
        import numpy as np
        import math
        D = 256
        B, L = (8, 1024)
        EPS = 1e-05

        def layer_norm(y, gamma, beta):
            mu = jnp.mean(y, axis=-1, keepdims=True)
            var = jnp.mean(jnp.square(y - mu), axis=-1, keepdims=True)
            return (y - mu) * jax.lax.rsqrt(var + EPS) * gamma + beta
        key = jax.random.key(seed)
        ks = jax.random.split(key, 8)
        s = 1.0 / math.sqrt(D)
        x = jax.random.normal(ks[0], (B, L, D), dtype=jnp.float32)
        adj = jax.random.randint(ks[1], (B, L, L), 0, 2, dtype=jnp.int32)
        Wq = jax.random.normal(ks[2], (D, D), dtype=jnp.float32) * s
        Wk = jax.random.normal(ks[3], (D, D), dtype=jnp.float32) * s
        Wv = jax.random.normal(ks[4], (D, D), dtype=jnp.float32) * s
        Wo = jax.random.normal(ks[5], (D, D), dtype=jnp.float32) * s
        bo = jnp.zeros((D,), dtype=jnp.float32)
        gamma = jnp.ones((D,), dtype=jnp.float32)
        beta = jnp.zeros((D,), dtype=jnp.float32)
        return {'x': x, 'adj': adj, 'Wq': Wq, 'Wk': Wk, 'Wv': Wv, 'Wo': Wo, 'bo': bo, 'gamma': gamma, 'beta': beta}
    _L1_gnn_all = _L1_gnn_setup()
    _L1_gnn_in = {k: v for k, v in _L1_gnn_all.items() if k in ('Wq', 'Wk', 'Wv', 'Wo', 'bo', 'gamma', 'beta')}
    del _L1_gnn_all
    return {'x': x, 'adj': adj, 'L0_gnn_Wq': _L0_gnn_in['Wq'], 'L0_gnn_Wk': _L0_gnn_in['Wk'], 'L0_gnn_Wv': _L0_gnn_in['Wv'], 'L0_gnn_Wo': _L0_gnn_in['Wo'], 'L0_gnn_bo': _L0_gnn_in['bo'], 'L0_gnn_gamma': _L0_gnn_in['gamma'], 'L0_gnn_beta': _L0_gnn_in['beta'], 'L1_gnn_Wq': _L1_gnn_in['Wq'], 'L1_gnn_Wk': _L1_gnn_in['Wk'], 'L1_gnn_Wv': _L1_gnn_in['Wv'], 'L1_gnn_Wo': _L1_gnn_in['Wo'], 'L1_gnn_bo': _L1_gnn_in['bo'], 'L1_gnn_gamma': _L1_gnn_in['gamma'], 'L1_gnn_beta': _L1_gnn_in['beta']}

def reference(x, adj, L0_gnn_Wq, L0_gnn_Wk, L0_gnn_Wv, L0_gnn_Wo, L0_gnn_bo, L0_gnn_gamma, L0_gnn_beta, L1_gnn_Wq, L1_gnn_Wk, L1_gnn_Wv, L1_gnn_Wo, L1_gnn_bo, L1_gnn_gamma, L1_gnn_beta):
    import jax
    import jax.numpy as jnp

    def _L0_gnn_ref(x, adj, Wq, Wk, Wv, Wo, bo, gamma, beta):
        import jax, jax.numpy as jnp
        import numpy as np
        import math
        D = 256
        B, L = (8, 1024)
        EPS = 1e-05

        def layer_norm(y, gamma, beta):
            mu = jnp.mean(y, axis=-1, keepdims=True)
            var = jnp.mean(jnp.square(y - mu), axis=-1, keepdims=True)
            return (y - mu) * jax.lax.rsqrt(var + EPS) * gamma + beta
        d_out = Wq.shape[1]
        scale = 1.0 / math.sqrt(d_out)
        Q = x @ Wq
        K = x @ Wk
        V = x @ Wv
        sc = jnp.einsum('bld,bmd->blm', Q, K) * scale
        mask = adj == 0
        sc = jnp.where(mask, -jnp.inf, sc)
        all_inf = jnp.all(mask, axis=-1, keepdims=True)
        sc = jnp.where(all_inf, 0.0, sc)
        w = jax.nn.softmax(sc, axis=-1)
        out = jnp.einsum('blm,bmd->bld', w, V)
        y = x + out @ Wo + bo
        return layer_norm(y, gamma, beta)

    def _L1_gnn_ref(x, adj, Wq, Wk, Wv, Wo, bo, gamma, beta):
        import jax, jax.numpy as jnp
        import numpy as np
        import math
        D = 256
        B, L = (8, 1024)
        EPS = 1e-05

        def layer_norm(y, gamma, beta):
            mu = jnp.mean(y, axis=-1, keepdims=True)
            var = jnp.mean(jnp.square(y - mu), axis=-1, keepdims=True)
            return (y - mu) * jax.lax.rsqrt(var + EPS) * gamma + beta
        d_out = Wq.shape[1]
        scale = 1.0 / math.sqrt(d_out)
        Q = x @ Wq
        K = x @ Wk
        V = x @ Wv
        sc = jnp.einsum('bld,bmd->blm', Q, K) * scale
        mask = adj == 0
        sc = jnp.where(mask, -jnp.inf, sc)
        all_inf = jnp.all(mask, axis=-1, keepdims=True)
        sc = jnp.where(all_inf, 0.0, sc)
        w = jax.nn.softmax(sc, axis=-1)
        out = jnp.einsum('blm,bmd->bld', w, V)
        y = x + out @ Wo + bo
        return layer_norm(y, gamma, beta)
    x = _L0_gnn_ref(x, adj, L0_gnn_Wq, L0_gnn_Wk, L0_gnn_Wv, L0_gnn_Wo, L0_gnn_bo, L0_gnn_gamma, L0_gnn_beta)
    x = _L1_gnn_ref(x, adj, L1_gnn_Wq, L1_gnn_Wk, L1_gnn_Wv, L1_gnn_Wo, L1_gnn_bo, L1_gnn_gamma, L1_gnn_beta)
    return x

_drawn_inputs = setup_inputs


def setup_inputs(seed=0):
    import zlib

    import numpy as np

    out = dict(_drawn_inputs(seed))
    spreads = {'L0_gnn_bo': (0.0, 0.1),
     'L0_gnn_gamma': (1.0, 0.2),
     'L0_gnn_beta': (0.0, 0.1),
     'L1_gnn_bo': (0.0, 0.1),
     'L1_gnn_gamma': (1.0, 0.2),
     'L1_gnn_beta': (0.0, 0.1)}
    factors = {}
    for name, (base, spread) in spreads.items():
        noise = np.random.default_rng([zlib.crc32(name.encode()), seed]).standard_normal(out[name].shape)
        drawn = base * np.exp(spread * noise) if base else spread * noise
        out[name] = jnp.asarray(drawn.astype(out[name].dtype))
    for name, factor in factors.items():
        out[name] = (out[name] * factor).astype(out[name].dtype)
    return out
```

```python
from contextlib import ExitStack

import concourse.bass as bass
from concourse import mybir

F32 = mybir.dt.float32
F32R = mybir.dt.float32r
BF16 = mybir.dt.bfloat16
I32 = mybir.dt.int32
ALU = mybir.AluOpType
ACT = mybir.ActivationFunctionType

P = 128
EPS = 1e-5
MASKED = 2.0 ** 127

LAYERS = 2
DMA = 16


class Item:

    def __init__(self, layer, n, b, n2, b2, b4, round):
        self.layer, self.n, self.b = layer, n, b
        self.n2, self.b2, self.b4, self.round = n2, b2, b4, round


def item_order(graphs):
    order = [(0, 0), (0, 1), (0, 2), (0, 3), (1, 0), (1, 1)]
    for b in range(4, graphs - 2):
        order += [(0, b), (1, b - 2)]
    return order + [(0, graphs - 2), (0, graphs - 1)] + [(1, b) for b in range(graphs - 4, graphs)]


def gnn_two_layers(nc, x, adj, weights, out):
    B, L, D = x.shape
    LC, DC = L // P, D // P
    assert (LC, DC) == (2, 2)
    ORDER = item_order(B)
    ITEMS = len(ORDER)
    POS = {pair: k for k, pair in enumerate(ORDER)}
    FIRST, BODY = 8, 8
    TURNS = (ITEMS - FIRST - 8) // BODY
    assert all(ORDER[k + BODY * t] == (ORDER[k][0], ORDER[k][1] + BODY // 2 * t)
               for k in range(FIRST - 2, FIRST + BODY + 1) for t in range(TURNS))
    DRAIN = 2
    SCALE = -1.0 / float(D) ** 0.5
    ROOT_D = float(D) ** 0.5

    def item(k, turn):
        if not 0 <= k < ITEMS:
            return None
        layer, b = ORDER[k]
        return Item(layer, n=turn * BODY + k, b=turn * (BODY // 2) + b, n2=k % 2, b2=b % 2, b4=b % 4,
                    round=turn + b // 4)

    def wait_items(eng, sem, it, lag=0):
        if isinstance(it.n, int) and it.n - lag + 1 <= 0:
            return
        eng.wait_ge(sem, it.n + (1 - lag))

    def run_slots(eng, slot):
        for k in range(FIRST):
            slot(k, 0)
        with eng.Fori(0, TURNS) as turn:
            for k in range(FIRST, FIRST + BODY):
                slot(k, turn)
        for k in range(FIRST + BODY * TURNS, ITEMS + DRAIN):
            slot(k, 0)

    with ExitStack() as ctx:
        def sb(name, shape, dt=F32):
            return ctx.enter_context(nc.sbuf_tensor(name, shape, dt))

        def bank(name):
            return ctx.enter_context(nc.psum_tensor(name, [P, 2, 256], F32))

        def sem(name):
            return ctx.enter_context(nc.semaphore(name))

        ident = sb("ident", [P, P])
        minus_half = sb("minus_half", [P, LC])
        d_eps = sb("d_eps", [P, LC])
        a_hi = [sb(f"a_hi{l}", [P, DC, D], F32R) for l in range(LAYERS)]
        a_lo = [sb(f"a_lo{l}", [P, DC, D], F32R) for l in range(LAYERS)]
        c_hi = [sb(f"c_hi{l}", [P, DC, D], F32R) for l in range(LAYERS)]
        c_lo = [sb(f"c_lo{l}", [P, DC, D], F32R) for l in range(LAYERS)]
        bo = [sb(f"bo{l}", [P, LC, D]) for l in range(LAYERS)]
        gamma = [sb(f"gamma{l}", [P, LC, D]) for l in range(LAYERS)]
        beta = [sb(f"beta{l}", [P, LC, D]) for l in range(LAYERS)]
        w_in = {(l, w): sb(f"w_{w}{l}", [P, DC, D]) for l in range(LAYERS) for w in ("Wq", "Wk", "Wv", "Wo")}
        w_t = {w: sb(f"wt_{w}", [P, DC, D]) for w in ("Wq", "Wk", "Wv")}
        x_in = [sb(f"x_in{i}", [P, LC, D]) for i in range(4)]
        adj_in = [sb(f"adj_in{i}", [P, LC, L], I32) for i in range(4)]
        mask = [sb(f"mask{i}", [P, LC, L], BF16) for i in range(4)]
        x_mid = [sb(f"x_mid{i}", [P, LC, D]) for i in range(2)]
        x_out = sb("x_out", [P, LC, D])
        xt_hi = [sb(f"xt_hi{i}", [P, DC, L], F32R) for i in range(2)]
        xt_lo = [sb(f"xt_lo{i}", [P, DC, L], F32R) for i in range(2)]
        g_hi = sb("g_hi", [P, DC, L], F32R)
        g_lo = sb("g_lo", [P, DC, L], F32R)
        v_hi = [sb(f"v_hi{i}", [P, LC, D], F32R) for i in range(2)]
        v_lo = [sb(f"v_lo{i}", [P, LC, D], F32R) for i in range(2)]
        prob = sb("prob", [P, LC, L])
        pt_hi = sb("pt_hi", [P, LC, L], F32R)
        pt_lo = sb("pt_lo", [P, LC, L], F32R)
        x_bias = [sb(f"x_bias{i}", [P, LC, D]) for i in range(2)]
        y = [sb(f"y{i}", [P, LC, D]) for i in range(2)]
        centred = [sb(f"centred{i}", [P, LC, D]) for i in range(2)]
        normal = [sb(f"normal{i}", [P, LC, D]) for i in range(2)]
        square = [sb(f"square{i}", [P, LC, D]) for i in range(2)]
        neg_max = [sb(f"neg_max{i}", [P, LC]) for i in range(2)]
        row_sum = [sb(f"row_sum{i}", [P, LC]) for i in range(2)]
        row_inv = [sb(f"row_inv{i}", [P, LC]) for i in range(2)]
        y_sum = [sb(f"y_sum{i}", [P, LC]) for i in range(2)]
        neg_mean = [sb(f"neg_mean{i}", [P, LC]) for i in range(2)]
        square_sum = [sb(f"square_sum{i}", [P, LC]) for i in range(2)]
        var_eps = [sb(f"var_eps{i}", [P, LC]) for i in range(2)]
        rstd = [sb(f"rstd{i}", [P, LC]) for i in range(2)]

        ps_xt, ps_g, ps_v, ps_s, ps_pt, ps_o, ps_w0, ps_w1 = (
            bank(n) for n in ("ps_xt", "ps_g", "ps_v", "ps_s", "ps_pt", "ps_o", "ps_w0", "ps_w1"))
        ps_w = [ps_w0, ps_w1]

        w_loaded = [sem(f"w_loaded{l}") for l in range(LAYERS)]
        vec_loaded = sem("vec_loaded")
        x_loaded = [sem(f"x_loaded{i}") for i in range(4)]
        adj_loaded = [sem(f"adj_loaded{i}") for i in range(4)]
        stored = sem("stored")
        ident_zero, ident_done, consts_done, gamma_done = (
            sem(n) for n in ("ident_zero", "ident_done", "consts_done", "gamma_done"))
        w_psum, w_copied, w_hi_done, w_lo_done = (sem(n) for n in ("w_psum", "w_copied", "w_hi_done", "w_lo_done"))
        xt_psum, g_psum, v_psum, s_psum, pt_psum, o_psum = (
            sem(n) for n in ("xt_psum", "g_psum", "v_psum", "s_psum", "pt_psum", "o_psum"))
        xt_hi_done, g_hi_done, v_hi_done, pt_hi_done = (
            sem(n) for n in ("xt_hi_done", "g_hi_done", "v_hi_done", "pt_hi_done"))
        xt_lo_done, g_lo_done, v_lo_done, pt_lo_done = (
            sem(n) for n in ("xt_lo_done", "g_lo_done", "v_lo_done", "pt_lo_done"))
        s_masked, prob_done, inv_done, y_done, mean_done, square_done = (
            sem(n) for n in ("s_masked", "prob_done", "inv_done", "y_done", "mean_done", "square_done"))
        x_bias_done, centred_done, var_done, rstd_done, normal_done = (
            sem(n) for n in ("x_bias_done", "centred_done", "var_done", "rstd_done", "normal_done"))
        mask_done, mid_done, out_done = sem("mask_done"), sem("mid_done"), sem("out_done")

        x_rows = x.rearrange("b (c p) d -> b p c d", p=P)
        adj_rows = adj.rearrange("b (c p) m -> b p c m", p=P)
        out_rows = out.rearrange("b (c p) d -> b p c d", p=P)

        block = ctx.enter_context(nc.Block())

        @block.sync
        def _(sp):
            def load_x(b, slot):
                sp.dma_start(x_in[slot][:], x_rows[b]).then_inc(x_loaded[slot], DMA)

            def load_adj(b, slot):
                sp.dma_start(adj_in[slot][:], adj_rows[b]).then_inc(adj_loaded[slot], DMA)

            def load_weights(l):
                for w in ("Wq", "Wk", "Wv", "Wo"):
                    sp.dma_start(w_in[l, w][:], weights[l, w].rearrange("(c p) n -> p c n", p=P)
                                 ).then_inc(w_loaded[l], DMA)

            load_weights(0)
            load_x(0, 0)
            load_adj(0, 0)
            load_weights(1)
            for l in range(LAYERS):
                for tile, name in ((bo, "bo"), (gamma, "gamma"), (beta, "beta")):
                    for c in range(LC):
                        sp.dma_start(tile[l][:, c, :], weights[l, name].partition_broadcast(P)
                                     ).then_inc(vec_loaded, DMA)
            for b in range(1, 4):
                load_x(b, b)
                load_adj(b, b)

            def slot(k, turn):
                old = item(k - 2, turn)
                if old is not None and old.layer == 0 and ORDER[k - 2][1] + 4 < B:
                    wait_items(sp, xt_psum, old)
                    wait_items(sp, x_bias_done, old)
                    load_x(old.b + 4, old.b4)
                    sp.wait_ge(mask_done, old.b + 1)
                    load_adj(old.b + 4, old.b4)
                if old is not None and old.layer == 1:
                    sp.wait_ge(out_done, old.b + 1)
                    sp.dma_start(out_rows[old.b], x_out[:]).then_inc(stored, DMA)

            run_slots(sp, slot)
            sp.wait_ge(stored, DMA * B)

        @block.tensor
        def _(pe):
            def transpose4(dst, src):
                for f in range(2):
                    for r in range(2):
                        last = nc.tensor.transpose(dst[:, f, r * P:(r + 1) * P], src[:, r, f * P:(f + 1) * P],
                                                   ident[:])
                return last

            def product(dst, lhs_hi, lhs_lo, rhs_hi, rhs_lo):
                for r in range(2):
                    rows = slice(r * P, (r + 1) * P)
                    terms = [(h, g, f) for f in range(2)
                             for h, g in ((lhs_lo, rhs_hi), (lhs_hi, rhs_lo), (lhs_hi, rhs_hi))]
                    for i, (h, g, f) in enumerate(terms):
                        last = nc.tensor.matmul(dst[:, r, :], h[:, f, rows], g[:, f, :],
                                                start=(i == 0), stop=(i == len(terms) - 1))
                return last

            pe.wait_ge(ident_done, 1)

            def bank_of_step(step):
                l, i = divmod(step - 2, 5)
                if i < 3 and step >= 2:
                    pe.wait_ge(w_copied, 3 * l + i + 1)
                elif step >= 2:
                    pe.wait_ge(w_lo_done, 2 * l + i - 2)
                return ps_w[step % 2]

            for l in range(LAYERS):
                pe.wait_ge(w_loaded[l], 4 * DMA)
                for i, w in enumerate(("Wq", "Wk", "Wv")):
                    transpose4(bank_of_step(5 * l + i), w_in[l, w]).then_inc(w_psum, 1)
                for i, lhs, rhs, copies in ((3, w_t["Wq"], w_t["Wk"], 2), (4, w_t["Wv"], w_in[l, "Wo"], 3)):
                    dst = bank_of_step(5 * l + i)
                    pe.wait_ge(w_copied, 3 * l + copies)
                    for r in range(2):
                        for f in range(2):
                            last = nc.tensor.matmul(dst[:, r, :], lhs[:, f, r * P:(r + 1) * P], rhs[:, f, :],
                                                    start=(f == 0), stop=(f == 1))
                    last.then_inc(w_psum, 1)

            def transpose_x(it):
                if it.layer == 0:
                    pe.wait_ge(x_loaded[it.b4], it.round * DMA + DMA)
                else:
                    pe.wait_ge(mid_done, it.b + 1)
                wait_items(pe, xt_lo_done, it, lag=1)
                transpose4(ps_xt, x_in[it.b4] if it.layer == 0 else x_mid[it.b2]).then_inc(xt_psum, 1)

            def slot(k, turn):
                it, before, after = item(k, turn), item(k - 1, turn), item(k + 1, turn)
                if it is not None:
                    xh, xl = xt_hi[it.n2], xt_lo[it.n2]
                    wait_items(pe, xt_lo_done, it)
                    product(ps_g, a_hi[it.layer], a_lo[it.layer], xh, xl).then_inc(g_psum, 1)
                if before is not None:
                    wait_items(pe, prob_done, before)
                    transpose4(ps_pt, prob).then_inc(pt_psum, 1)
                if after is not None:
                    transpose_x(after)
                if it is not None:
                    wait_items(pe, v_lo_done, it, lag=1)
                    product(ps_v, xh, xl, c_hi[it.layer], c_lo[it.layer]).then_inc(v_psum, 1)
                    wait_items(pe, g_lo_done, it)
                    product(ps_s, g_hi, g_lo, xh, xl).then_inc(s_psum, 1)
                if before is not None:
                    wait_items(pe, pt_lo_done, before)
                    wait_items(pe, v_lo_done, before)
                    wait_items(pe, y_done, before, lag=1)
                    product(ps_o, pt_hi, pt_lo, v_hi[before.n2], v_lo[before.n2]).then_inc(o_psum, 1)

            pe.wait_ge(w_lo_done, 2 * LAYERS)
            transpose_x(item(0, 0))
            run_slots(pe, lambda k, turn: slot(k, turn) if k <= ITEMS else None)

        @block.scalar
        def _(act):
            for l in range(LAYERS):
                act.wait_ge(w_psum, 5 * l + 4)
                nc.scalar.activation(a_hi[l][:], ps_w[(5 * l + 3) % 2][:], ACT.Copy, scale=SCALE).then_inc(w_hi_done, 1)
                act.wait_ge(w_psum, 5 * l + 5)
                nc.scalar.activation(c_hi[l][:], ps_w[(5 * l + 4) % 2][:], ACT.Copy).then_inc(w_hi_done, 1)

            def high_half(it, psum_ready, dst, src, done):
                wait_items(act, psum_ready, it)
                nc.scalar.activation(dst[:], src[:], ACT.Copy).then_inc(done, 1)

            def slot(k, turn):
                it, before, after, old = (item(k + d, turn) for d in (0, -1, 1, -2))
                if it is not None:
                    high_half(it, g_psum, g_hi, ps_g, g_hi_done)
                if before is not None:
                    high_half(before, pt_psum, pt_hi, ps_pt, pt_hi_done)
                if after is not None:
                    high_half(after, xt_psum, xt_hi[after.n2], ps_xt, xt_hi_done)
                if old is not None:
                    wait_items(act, mean_done, old)
                    for c in range(LC):
                        last = nc.scalar.activation(square[old.n2][:, c, :], y[old.n2][:, c, :], ACT.Square,
                                                    bias=neg_mean[old.n2][:, c:c + 1],
                                                    accum_out=square_sum[old.n2][:, c:c + 1])
                    last.then_inc(square_done, 1)
                if it is not None:
                    high_half(it, v_psum, v_hi[it.n2], ps_v, v_hi_done)
                    wait_items(act, s_masked, it)
                    for c in range(LC):
                        last = nc.scalar.activation(prob[:, c, :], ps_s[:, c, :], ACT.Exp, scale=-1.0,
                                                    bias=neg_max[it.n2][:, c:c + 1],
                                                    accum_out=row_sum[it.n2][:, c:c + 1])
                    last.then_inc(prob_done, 1)

            high_half(item(0, 0), xt_psum, xt_hi[0], ps_xt, xt_hi_done)
            run_slots(act, slot)

        @block.vector
        def _(dve):
            nc.vector.memset(minus_half[:], -0.5).then_inc(consts_done, 1)
            nc.vector.memset(d_eps[:], D * EPS).then_inc(consts_done, 1)
            for l in range(LAYERS):
                for i, w in enumerate(("Wq", "Wk", "Wv")):
                    dve.wait_ge(w_psum, 5 * l + i + 1)
                    nc.vector.tensor_copy(w_t[w][:], ps_w[(5 * l + i) % 2][:]).then_inc(w_copied, 1)
                for i, (hi, lo, s) in enumerate(((a_hi, a_lo, SCALE), (c_hi, c_lo, 1.0))):
                    dve.wait_ge(w_hi_done, 2 * l + i + 1)
                    nc.vector.scalar_tensor_tensor(lo[l][:], ps_w[(5 * l + 3 + i) % 2][:], s,
                                                   hi[l][:].bitcast(F32), ALU.mult, ALU.subtract).then_inc(w_lo_done, 1)

            def low_half(it, hi_done, dst, src, hi, done):
                wait_items(dve, hi_done, it)
                nc.vector.tensor_tensor(dst[:], src[:], hi[:].bitcast(F32), ALU.subtract).then_inc(done, 1)

            def slot(k, turn):
                it, before, after, old = (item(k + d, turn) for d in (0, -1, 1, -2))
                if old is not None:
                    wait_items(dve, square_done, old, lag=2)
                    wait_items(dve, inv_done, old)
                    wait_items(dve, o_psum, old)
                    wait_items(dve, x_bias_done, old)
                    for c in range(LC):
                        last = nc.vector.scalar_tensor_tensor(y[old.n2][:, c, :], ps_o[:, c, :],
                                                              row_inv[old.n2][:, c:c + 1], x_bias[old.n2][:, c, :],
                                                              ALU.mult, ALU.add, accum_out=y_sum[old.n2][:, c:c + 1])
                    last.then_inc(y_done, 1)
                    wait_items(dve, y_done, old)
                    nc.vector.tensor_scalar(neg_mean[old.n2][:], y_sum[old.n2][:], -1.0 / D, None,
                                            ALU.mult).then_inc(mean_done, 1)
                    wait_items(dve, normal_done, old, lag=2)
                    wait_items(dve, mean_done, old)
                    for c in range(LC):
                        last = nc.vector.scalar_tensor_tensor(centred[old.n2][:, c, :], y[old.n2][:, c, :],
                                                              neg_mean[old.n2][:, c:c + 1], gamma[old.layer][:, c, :],
                                                              ALU.add, ALU.mult)
                    last.then_inc(centred_done, 1)
                if it is not None:
                    low_half(it, g_hi_done, g_lo, ps_g, g_hi, g_lo_done)
                if before is not None:
                    low_half(before, pt_hi_done, pt_lo, ps_pt, pt_hi, pt_lo_done)
                if after is not None:
                    low_half(after, xt_hi_done, xt_lo[after.n2], ps_xt, xt_hi[after.n2], xt_lo_done)
                if it is not None:
                    wait_items(dve, s_psum, it)
                    dve.wait_ge(mask_done, it.b + 1)
                if before is not None:
                    nc.vector.reciprocal(row_inv[before.n2][:], row_sum[before.n2][:]).then_inc(inv_done, 1)
                if it is not None:
                    for c in range(LC):
                        last = nc.vector.tensor_tensor_reduce(out=ps_s[:, c, :], in0=ps_s[:, c, :],
                                                              in1=mask[it.b4][:, c, :], scale=1.0, scalar=3.0e38,
                                                              op0=ALU.add, op1=ALU.min,
                                                              accum_out=neg_max[it.n2][:, c:c + 1])
                    last.then_inc(s_masked, 1)
                    low_half(it, v_hi_done, v_lo[it.n2], ps_v, v_hi[it.n2], v_lo_done)
                if after is not None and after.layer == 0:
                    make_mask(after)

            def make_mask(it):
                dve.wait_ge(adj_loaded[it.b4], it.round * DMA + DMA)
                nc.vector.tensor_scalar(mask[it.b4][:], adj_in[it.b4][:], 0.0, MASKED, ALU.is_equal,
                                        ALU.mult).then_inc(mask_done, 1)

            make_mask(item(0, 0))
            low_half(item(0, 0), xt_hi_done, xt_lo[0], ps_xt, xt_hi[0], xt_lo_done)
            run_slots(dve, slot)

        @block.gpsimd
        def _(pool):
            nc.gpsimd.memset(ident[:], 0.0).then_inc(ident_zero, 1)
            pool.wait_ge(ident_zero, 1)
            nc.gpsimd.affine_select(out=ident[:], in_=ident[:], compare_op=ALU.not_equal, fill=1.0, base=0,
                                    pattern=[[-1, P]], channel_multiplier=1).then_inc(ident_done, 1)

            pool.wait_ge(vec_loaded, 6 * LC * DMA)
            for l in range(LAYERS):
                nc.gpsimd.tensor_scalar(gamma[l][:], gamma[l][:], ROOT_D, None, ALU.mult).then_inc(gamma_done, 1)
            pool.wait_ge(gamma_done, LAYERS)
            pool.wait_ge(consts_done, 2)

            def slot(k, turn):
                it, old = item(k, turn), item(k - 2, turn)
                if old is not None:
                    wait_items(pool, square_done, old)
                    nc.gpsimd.tensor_tensor(var_eps[old.n2][:], square_sum[old.n2][:], d_eps[:],
                                            ALU.add).then_inc(var_done, 1)
                    wait_items(pool, var_done, old)
                    nc.gpsimd.tensor_tensor(rstd[old.n2][:], var_eps[old.n2][:], minus_half[:],
                                            ALU.pow).then_inc(rstd_done, 1)
                if it is not None:
                    if it.layer == 0:
                        pool.wait_ge(x_loaded[it.b4], it.round * DMA + DMA)
                    else:
                        pool.wait_ge(mid_done, it.b + 1)
                    wait_items(pool, y_done, it, lag=2)
                    src = x_in[it.b4] if it.layer == 0 else x_mid[it.b2]
                    nc.gpsimd.tensor_tensor(x_bias[it.n2][:], src[:], bo[it.layer][:],
                                            ALU.add).then_inc(x_bias_done, 1)
                if old is not None:
                    z = normal[old.n2]
                    wait_items(pool, rstd_done, old)
                    wait_items(pool, centred_done, old)
                    nc.gpsimd.tensor_tensor(z[:], centred[old.n2][:],
                                            rstd[old.n2][:].unsqueeze(2).to_broadcast([P, LC, D]),
                                            ALU.mult).then_inc(normal_done, 1)
                    wait_items(pool, normal_done, old)
                    if old.layer == 0:
                        if (1, ORDER[k - 2][1] - 2) in POS:
                            wait_items(pool, xt_psum, old, lag=k - 2 - POS[1, ORDER[k - 2][1] - 2])
                        nc.gpsimd.tensor_tensor(x_mid[old.b2][:], z[:], beta[0][:], ALU.add).then_inc(mid_done, 1)
                    else:
                        if not isinstance(old.b, int) or old.b > 0:
                            pool.wait_ge(stored, old.b * DMA)
                        nc.gpsimd.tensor_tensor(x_out[:], z[:], beta[1][:], ALU.add).then_inc(out_done, 1)

            run_slots(pool, slot)


_WEIGHTS = ["Wq", "Wk", "Wv", "Wo", "bo", "gamma", "beta"]


def kernel(**inputs):
    import numpy as _np
    import concourse.bacc as _bacc
    from concourse import mybir as _mybir
    from concourse.bass_utils import run_bass_kernel_spmd as _run

    nc = _bacc.Bacc("TRN2", target_bir_lowering=False, num_devices=1)
    arrays = {}

    def dram_in(name):
        a = _np.ascontiguousarray(inputs[name])
        arrays[f"in_{name}_dram"] = a
        return nc.dram_tensor(f"in_{name}_dram", a.shape, _mybir.dt.from_np(a.dtype), kind="ExternalInput").ap()

    x, adj = dram_in("x"), dram_in("adj")
    weights = {(l, w): dram_in(f"L{l}_gnn_{w}") for l in range(LAYERS) for w in _WEIGHTS}
    out = nc.dram_tensor("out_dram", inputs["x"].shape, _mybir.dt.float32, kind="ExternalOutput").ap()
    gnn_two_layers(nc, x, adj, weights, out)
    r = _run(nc, [arrays], core_ids=[0])
    return r.results[0]["out_dram"]
```

```python
from contextlib import ExitStack

import concourse.bass as bass
from concourse import mybir

F32 = mybir.dt.float32
F32R = mybir.dt.float32r
BF16 = mybir.dt.bfloat16
I32 = mybir.dt.int32
ALU = mybir.AluOpType
ACT = mybir.ActivationFunctionType

P = 128
EPS = 1e-5
MASKED = 2.0 ** 127

LAYERS = 2
FACTORS = ("WqT", "WkT", "WvT", "Wo")
WARM_UP = 5
DMA = 16


class Item:

    def __init__(self, layer, n, b, n2, b2, b4, round):
        self.layer, self.n, self.b = layer, n, b
        self.n2, self.b2, self.b4, self.round = n2, b2, b4, round


def item_order(graphs):
    order = [(0, 0), (0, 1), (0, 2), (0, 3), (1, 0), (1, 1)]
    for b in range(4, graphs - 2):
        order += [(0, b), (1, b - 2)]
    return order + [(0, graphs - 2), (0, graphs - 1)] + [(1, b) for b in range(graphs - 4, graphs)]


def gnn_two_layers(nc, x, x_t, adj, weights, out):
    B, L, D = x.shape
    LC, DC = L // P, D // P
    assert (LC, DC) == (2, 2)
    ORDER = item_order(B)
    ITEMS = len(ORDER)
    POS = {pair: k for k, pair in enumerate(ORDER)}
    FIRST, BODY = 8, 8
    TURNS = (ITEMS - FIRST - 8) // BODY
    assert all(ORDER[k + BODY * t] == (ORDER[k][0], ORDER[k][1] + BODY // 2 * t)
               for k in range(FIRST - 2, FIRST + BODY + 1) for t in range(TURNS))
    DRAIN = 2
    SCALE = -1.0 / float(D) ** 0.5
    ROOT_D = float(D) ** 0.5

    def item(k, turn):
        if not 0 <= k < ITEMS:
            return None
        layer, b = ORDER[k]
        return Item(layer, n=turn * BODY + k, b=turn * (BODY // 2) + b, n2=k % 2, b2=b % 2, b4=b % 4,
                    round=turn + b // 4)

    def wait_items(eng, sem, it, lag=0):
        if isinstance(it.n, int) and it.n - lag + 1 <= 0:
            return
        eng.wait_ge(sem, it.n + (1 - lag))

    def run_slots(eng, slot):
        for k in range(FIRST):
            slot(k, 0)
        with eng.Fori(0, TURNS) as turn:
            for k in range(FIRST, FIRST + BODY):
                slot(k, turn)
        for k in range(FIRST + BODY * TURNS, ITEMS + DRAIN):
            slot(k, 0)

    with ExitStack() as ctx:
        def sb(name, shape, dt=F32):
            return ctx.enter_context(nc.sbuf_tensor(name, shape, dt))

        def bank(name):
            return ctx.enter_context(nc.psum_tensor(name, [P, 2, 256], F32))

        def sem(name):
            return ctx.enter_context(nc.semaphore(name))

        ident = sb("ident", [P, P])
        minus_half = sb("minus_half", [P, LC])
        d_eps = sb("d_eps", [P, LC])
        a_hi = [sb(f"a_hi{l}", [P, DC, D], F32R) for l in range(LAYERS)]
        a_lo = [sb(f"a_lo{l}", [P, DC, D], F32R) for l in range(LAYERS)]
        c_hi = [sb(f"c_hi{l}", [P, DC, D], F32R) for l in range(LAYERS)]
        c_lo = [sb(f"c_lo{l}", [P, DC, D], F32R) for l in range(LAYERS)]
        bo = [sb(f"bo{l}", [P, D]) for l in range(LAYERS)]
        gamma = [sb(f"gamma{l}", [P, D]) for l in range(LAYERS)]
        beta = [sb(f"beta{l}", [P, D]) for l in range(LAYERS)]
        w_in = {(l, w): sb(f"w_{w}{l}", [P, DC, D]) for l in range(LAYERS) for w in FACTORS}
        xt_in = [sb(f"xt_in{i}", [P, DC, L]) for i in range(4)]
        x_in = [sb(f"x_in{i}", [P, LC, D]) for i in range(4)]
        adj_in = [sb(f"adj_in{i}", [P, LC, L], I32) for i in range(4)]
        mask = [sb(f"mask{i}", [P, LC, L], BF16) for i in range(4)]
        x_mid = [sb(f"x_mid{i}", [P, LC, D]) for i in range(2)]
        x_out = sb("x_out", [P, LC, D])
        xt_hi = [sb(f"xt_hi{i}", [P, DC, L], F32R) for i in range(2)]
        xt_lo = [sb(f"xt_lo{i}", [P, DC, L], F32R) for i in range(2)]
        g_hi = sb("g_hi", [P, DC, L], F32R)
        g_lo = sb("g_lo", [P, DC, L], F32R)
        v_hi = [sb(f"v_hi{i}", [P, LC, D], F32R) for i in range(2)]
        v_lo = [sb(f"v_lo{i}", [P, LC, D], F32R) for i in range(2)]
        prob = sb("prob", [P, LC, L])
        pt_hi = sb("pt_hi", [P, LC, L], F32R)
        pt_lo = sb("pt_lo", [P, LC, L], F32R)
        x_bias = [sb(f"x_bias{i}", [P, LC, D]) for i in range(2)]
        y = [sb(f"y{i}", [P, LC, D]) for i in range(2)]
        centred = [sb(f"centred{i}", [P, LC, D]) for i in range(2)]
        normal = [sb(f"normal{i}", [P, LC, D]) for i in range(2)]
        square = [sb(f"square{i}", [P, LC, D]) for i in range(2)]
        neg_max = [sb(f"neg_max{i}", [P, LC]) for i in range(2)]
        row_sum = [sb(f"row_sum{i}", [P, LC]) for i in range(2)]
        row_inv = [sb(f"row_inv{i}", [P, LC]) for i in range(2)]
        y_sum = [sb(f"y_sum{i}", [P, LC]) for i in range(2)]
        neg_mean = [sb(f"neg_mean{i}", [P, LC]) for i in range(2)]
        square_sum = [sb(f"square_sum{i}", [P, LC]) for i in range(2)]
        var_eps = [sb(f"var_eps{i}", [P, LC]) for i in range(2)]
        rstd = [sb(f"rstd{i}", [P, LC]) for i in range(2)]

        ps_xt, ps_g, ps_v, ps_s, ps_pt, ps_o, ps_w0, ps_w1 = (
            bank(n) for n in ("ps_xt", "ps_g", "ps_v", "ps_s", "ps_pt", "ps_o", "ps_w0", "ps_w1"))
        ps_w = [ps_w0, ps_w1]

        qk_loaded = [sem(f"qk_loaded{l}") for l in range(LAYERS)]
        vo_loaded = [sem(f"vo_loaded{l}") for l in range(LAYERS)]
        vec_loaded = [sem(f"vec_loaded{l}") for l in range(LAYERS)]
        xt_loaded = [sem(f"xt_loaded{i}") for i in range(4)]
        x_loaded = [sem(f"x_loaded{i}") for i in range(4)]
        adj_loaded = [sem(f"adj_loaded{i}") for i in range(4)]
        stored = sem("stored")
        ident_zero, ident_done, consts_done, gamma_done = (
            sem(n) for n in ("ident_zero", "ident_done", "consts_done", "gamma_done"))
        w_psum, w_hi_done, w_lo_done = (sem(n) for n in ("w_psum", "w_hi_done", "w_lo_done"))
        g_psum, v_psum, s_psum, pt_psum, o_psum = (
            sem(n) for n in ("g_psum", "v_psum", "s_psum", "pt_psum", "o_psum"))
        xt_hi_done, g_hi_done, v_hi_done, pt_hi_done = (
            sem(n) for n in ("xt_hi_done", "g_hi_done", "v_hi_done", "pt_hi_done"))
        xt_lo_done, g_lo_done, v_lo_done, pt_lo_done = (
            sem(n) for n in ("xt_lo_done", "g_lo_done", "v_lo_done", "pt_lo_done"))
        s_masked, prob_done, inv_done, y_done, mean_done, square_done = (
            sem(n) for n in ("s_masked", "prob_done", "inv_done", "y_done", "mean_done", "square_done"))
        x_bias_done, centred_done, var_done, rstd_done, normal_done = (
            sem(n) for n in ("x_bias_done", "centred_done", "var_done", "rstd_done", "normal_done"))
        mask_done, xt_psum, mid_done, out_done = (sem(n) for n in ("mask_done", "xt_psum", "mid_done", "out_done"))
        last_done = sem("last_done")

        x_rows = x.rearrange("b (c p) d -> b p c d", p=P)
        xt_rows = x_t.rearrange("b (c p) l -> b p c l", p=P)
        adj_rows = adj.rearrange("b (c p) m -> b p c m", p=P)
        out_rows = out.rearrange("b (c p) d -> b p c d", p=P)

        block = ctx.enter_context(nc.Block())

        @block.sync
        def _(sp):
            def load(dst, src, loaded):
                sp.dma_start(dst[:], src).then_inc(loaded, DMA)

            def load_weight(l, w, loaded):
                load(w_in[l, w], weights[l, w].rearrange("(c p) n -> p c n", p=P), loaded[l])

            load_weight(0, "WqT", qk_loaded)
            load_weight(0, "WkT", qk_loaded)
            load(xt_in[0], xt_rows[0], xt_loaded[0])
            load_weight(0, "WvT", vo_loaded)
            load_weight(0, "Wo", vo_loaded)
            load(xt_in[1], xt_rows[1], xt_loaded[1])
            load(adj_in[0], adj_rows[0], adj_loaded[0])
            load(adj_in[1], adj_rows[1], adj_loaded[1])
            load(x_in[0], x_rows[0], x_loaded[0])
            for l in range(LAYERS):
                for tile, name in ((bo, "bo"), (gamma, "gamma"), (beta, "beta")):
                    load(tile[l], weights[l, name].partition_broadcast(P), vec_loaded[l])
                if l == 0:
                    for w in FACTORS:
                        load_weight(1, w, qk_loaded if w in ("WqT", "WkT") else vo_loaded)
                    load(x_in[1], x_rows[1], x_loaded[1])
                    for b in range(2, 4):
                        load(xt_in[b], xt_rows[b], xt_loaded[b])
                        load(adj_in[b], adj_rows[b], adj_loaded[b])
                        load(x_in[b], x_rows[b], x_loaded[b])

            def slot(k, turn):
                old = item(k - 2, turn)
                if old is not None and old.layer == 0 and ORDER[k - 2][1] + 4 < B:
                    wait_items(sp, xt_lo_done, old)
                    load(xt_in[old.b4], xt_rows[old.b + 4], xt_loaded[old.b4])
                    wait_items(sp, x_bias_done, old)
                    load(x_in[old.b4], x_rows[old.b + 4], x_loaded[old.b4])
                    sp.wait_ge(mask_done, old.b + 1)
                    load(adj_in[old.b4], adj_rows[old.b + 4], adj_loaded[old.b4])
                if old is not None and old.layer == 1 and k - 2 < ITEMS - 1:
                    sp.wait_ge(out_done, old.b + 1)
                    sp.dma_start(out_rows[old.b], x_out[:]).then_inc(stored, DMA)

            run_slots(sp, slot)
            sp.wait_ge(stored, DMA * (B - 1))
            for c in range(LC):
                sp.wait_ge(last_done, c + 1)
                sp.dma_start(out_rows[B - 1][:, c, :], x_out[:, c, :]).then_inc(stored, DMA)
            sp.wait_ge(stored, DMA * (B - 1 + LC))

        @block.tensor
        def _(pe):
            def transpose4(dst, src):
                for f in range(2):
                    for r in range(2):
                        last = nc.tensor.transpose(dst[:, f, r * P:(r + 1) * P], src[:, r, f * P:(f + 1) * P],
                                                   ident[:])
                return last

            def product(dst, lhs_hi, lhs_lo, rhs_hi, rhs_lo):
                for r in range(2):
                    rows = slice(r * P, (r + 1) * P)
                    terms = [(h, g, f) for f in range(2)
                             for h, g in ((lhs_lo, rhs_hi), (lhs_hi, rhs_lo), (lhs_hi, rhs_hi))]
                    for i, (h, g, f) in enumerate(terms):
                        last = nc.tensor.matmul(dst[:, r, :], h[:, f, rows], g[:, f, :],
                                                start=(i == 0), stop=(i == len(terms) - 1))
                return last

            def combine_weights(l, i):
                lhs, rhs, loaded = ("WqT", "WkT", qk_loaded) if i == 0 else ("WvT", "Wo", vo_loaded)
                pe.wait_ge(loaded[l], 2 * DMA)
                if l > 0:
                    pe.wait_ge(w_lo_done, 2 * (l - 1) + i + 1)
                for r in range(2):
                    for f in range(2):
                        last = nc.tensor.matmul(ps_w[i][:, r, :], w_in[l, lhs][:, f, r * P:(r + 1) * P],
                                                w_in[l, rhs][:, f, :], start=(f == 0), stop=(f == 1))
                last.then_inc(w_psum, 1)

            pe.wait_ge(ident_done, 1)
            for i in range(WARM_UP):
                nc.tensor.matmul(ps_xt[:, 0, 0:P], ident[:], ident[:], start=True, stop=True)
            combine_weights(0, 0)
            combine_weights(0, 1)

            def slot(k, turn):
                it, before, after = item(k, turn), item(k - 1, turn), item(k + 1, turn)
                if it is not None:
                    xh, xl = xt_hi[it.n2], xt_lo[it.n2]
                    if k == 0 or k == POS[1, 0]:
                        pe.wait_ge(w_lo_done, 1 if k == 0 else 2 * LAYERS)
                    wait_items(pe, xt_lo_done, it)
                    product(ps_g, a_hi[it.layer], a_lo[it.layer], xh, xl).then_inc(g_psum, 1)
                if k in (1, 2):
                    combine_weights(1, k - 1)
                if before is not None:
                    wait_items(pe, prob_done, before)
                    transpose4(ps_pt, prob).then_inc(pt_psum, 1)
                if after is not None and after.layer == 1:
                    pe.wait_ge(mid_done, after.b + 1)
                    transpose4(ps_xt, x_mid[after.b2]).then_inc(xt_psum, 1)
                if it is not None:
                    if k == 0:
                        pe.wait_ge(w_lo_done, 2)
                    wait_items(pe, v_lo_done, it, lag=1)
                    product(ps_v, xh, xl, c_hi[it.layer], c_lo[it.layer]).then_inc(v_psum, 1)
                    wait_items(pe, g_lo_done, it)
                    product(ps_s, g_hi, g_lo, xh, xl).then_inc(s_psum, 1)
                if before is not None:
                    wait_items(pe, pt_lo_done, before)
                    wait_items(pe, v_lo_done, before)
                    wait_items(pe, y_done, before, lag=1)
                    product(ps_o, pt_hi, pt_lo, v_hi[before.n2], v_lo[before.n2]).then_inc(o_psum, 1)

            run_slots(pe, slot)

        @block.scalar
        def _(act):
            def split_weights(l):
                act.wait_ge(w_psum, 2 * l + 1)
                nc.scalar.activation(a_hi[l][:], ps_w[0][:], ACT.Copy, scale=SCALE).then_inc(w_hi_done, 1)
                act.wait_ge(w_psum, 2 * l + 2)
                nc.scalar.activation(c_hi[l][:], ps_w[1][:], ACT.Copy).then_inc(w_hi_done, 1)

            def high_half(it, psum_ready, dst, src, done):
                wait_items(act, psum_ready, it)
                nc.scalar.activation(dst[:], src[:], ACT.Copy).then_inc(done, 1)

            def high_half_of_x(it):
                wait_items(act, s_psum, it, lag=2)
                if it.layer == 1:
                    act.wait_ge(xt_psum, it.b + 1)
                    src = ps_xt
                else:
                    act.wait_ge(xt_loaded[it.b4], it.round * DMA + DMA)
                    src = xt_in[it.b4]
                nc.scalar.activation(xt_hi[it.n2][:], src[:], ACT.Copy).then_inc(xt_hi_done, 1)

            def slot(k, turn):
                it, before, after, old = (item(k + d, turn) for d in (0, -1, 1, -2))
                if after is not None and after.layer == 0:
                    high_half_of_x(after)
                if it is not None:
                    high_half(it, g_psum, g_hi, ps_g, g_hi_done)
                if before is not None:
                    high_half(before, pt_psum, pt_hi, ps_pt, pt_hi_done)
                if old is not None:
                    wait_items(act, mean_done, old)
                    for c in range(LC):
                        last = nc.scalar.activation(square[old.n2][:, c, :], y[old.n2][:, c, :], ACT.Square,
                                                    bias=neg_mean[old.n2][:, c:c + 1],
                                                    accum_out=square_sum[old.n2][:, c:c + 1])
                    last.then_inc(square_done, 1)
                if after is not None and after.layer == 1:
                    high_half_of_x(after)
                if k == 2:
                    split_weights(1)
                if it is not None:
                    high_half(it, v_psum, v_hi[it.n2], ps_v, v_hi_done)
                    wait_items(act, s_masked, it)
                    for c in range(LC):
                        last = nc.scalar.activation(prob[:, c, :], ps_s[:, c, :], ACT.Exp, scale=-1.0,
                                                    bias=neg_max[it.n2][:, c:c + 1],
                                                    accum_out=row_sum[it.n2][:, c:c + 1])
                    last.then_inc(prob_done, 1)

            high_half_of_x(item(0, 0))
            split_weights(0)
            run_slots(act, slot)

        @block.vector
        def _(dve):
            nc.vector.memset(minus_half[:], -0.5).then_inc(consts_done, 1)
            nc.vector.memset(d_eps[:], D * EPS).then_inc(consts_done, 1)

            def split_weights(l):
                for i, (hi, lo, scale) in enumerate(((a_hi, a_lo, SCALE), (c_hi, c_lo, 1.0))):
                    dve.wait_ge(w_hi_done, 2 * l + i + 1)
                    nc.vector.scalar_tensor_tensor(lo[l][:], ps_w[i][:], scale, hi[l][:].bitcast(F32),
                                                   ALU.mult, ALU.subtract).then_inc(w_lo_done, 1)

            def low_half(it, hi_done, dst, src, hi, done):
                wait_items(dve, hi_done, it)
                nc.vector.tensor_tensor(dst[:], src[:], hi[:].bitcast(F32), ALU.subtract).then_inc(done, 1)

            def slot(k, turn):
                it, before, after, old = (item(k + d, turn) for d in (0, -1, 1, -2))
                if old is not None:
                    wait_items(dve, square_done, old, lag=2)
                    wait_items(dve, inv_done, old)
                    wait_items(dve, o_psum, old)
                    wait_items(dve, x_bias_done, old)
                    for c in range(LC):
                        last = nc.vector.scalar_tensor_tensor(y[old.n2][:, c, :], ps_o[:, c, :],
                                                              row_inv[old.n2][:, c:c + 1], x_bias[old.n2][:, c, :],
                                                              ALU.mult, ALU.add, accum_out=y_sum[old.n2][:, c:c + 1])
                    last.then_inc(y_done, 1)
                    wait_items(dve, y_done, old)
                    nc.vector.tensor_scalar(neg_mean[old.n2][:], y_sum[old.n2][:], -1.0 / D, None,
                                            ALU.mult).then_inc(mean_done, 1)
                if it is not None:
                    low_half(it, g_hi_done, g_lo, ps_g, g_hi, g_lo_done)
                if before is not None:
                    low_half(before, pt_hi_done, pt_lo, ps_pt, pt_hi, pt_lo_done)
                if old is not None:
                    wait_items(dve, normal_done, old, lag=2)
                    if k - 2 in (0, POS[1, 0]):
                        dve.wait_ge(gamma_done, ORDER[k - 2][0] + 1)
                    wait_items(dve, mean_done, old)
                    for c in range(LC):
                        last = nc.vector.scalar_tensor_tensor(centred[old.n2][:, c, :], y[old.n2][:, c, :],
                                                              neg_mean[old.n2][:, c:c + 1], gamma[old.layer][:],
                                                              ALU.add, ALU.mult)
                    last.then_inc(centred_done, 1)
                    if k - 2 == ITEMS - 1:
                        wait_items(dve, rstd_done, old)
                        wait_items(dve, centred_done, old)
                        dve.wait_ge(stored, old.b * DMA)
                        for c in range(LC):
                            nc.vector.scalar_tensor_tensor(x_out[:, c, :], centred[old.n2][:, c, :],
                                                           rstd[old.n2][:, c:c + 1], beta[1][:], ALU.mult,
                                                           ALU.add).then_inc(last_done, 1)
                if after is not None and after.layer == 1:
                    low_half(after, xt_hi_done, xt_lo[after.n2], ps_xt, xt_hi[after.n2], xt_lo_done)
                if k == 2:
                    split_weights(1)
                if it is not None:
                    wait_items(dve, s_psum, it)
                    dve.wait_ge(mask_done, it.b + 1)
                if before is not None:
                    nc.vector.reciprocal(row_inv[before.n2][:], row_sum[before.n2][:]).then_inc(inv_done, 1)
                if it is not None:
                    for c in range(LC):
                        last = nc.vector.tensor_tensor_reduce(out=ps_s[:, c, :], in0=ps_s[:, c, :],
                                                              in1=mask[it.b4][:, c, :], scale=1.0, scalar=3.0e38,
                                                              op0=ALU.add, op1=ALU.min,
                                                              accum_out=neg_max[it.n2][:, c:c + 1])
                    last.then_inc(s_masked, 1)
                    low_half(it, v_hi_done, v_lo[it.n2], ps_v, v_hi[it.n2], v_lo_done)
                if after is not None and after.layer == 0:
                    make_mask(after)

            def make_mask(it):
                dve.wait_ge(adj_loaded[it.b4], it.round * DMA + DMA)
                nc.vector.tensor_scalar(mask[it.b4][:], adj_in[it.b4][:], 0.0, MASKED, ALU.is_equal,
                                        ALU.mult).then_inc(mask_done, 1)

            split_weights(0)
            make_mask(item(0, 0))
            run_slots(dve, slot)

        @block.gpsimd
        def _(pool):
            nc.gpsimd.memset(ident[:], 0.0).then_inc(ident_zero, 1)
            pool.wait_ge(ident_zero, 1)
            nc.gpsimd.affine_select(out=ident[:], in_=ident[:], compare_op=ALU.not_equal, fill=1.0, base=0,
                                    pattern=[[-1, P]], channel_multiplier=1).then_inc(ident_done, 1)

            def scale_gamma(l):
                pool.wait_ge(vec_loaded[l], 3 * DMA)
                nc.gpsimd.tensor_scalar(gamma[l][:], gamma[l][:], ROOT_D, 0.0, ALU.mult,
                                        ALU.add).then_inc(gamma_done, 1)

            def per_row(tile):
                return tile[:].unsqueeze(1).to_broadcast([P, LC, D])

            def low_half_of_x(it):
                wait_items(pool, xt_hi_done, it)
                nc.gpsimd.tensor_tensor(xt_lo[it.n2][:], xt_in[it.b4][:], xt_hi[it.n2][:].bitcast(F32),
                                        ALU.subtract).then_inc(xt_lo_done, 1)

            low_half_of_x(item(0, 0))
            low_half_of_x(item(1, 0))
            scale_gamma(0)
            pool.wait_ge(consts_done, 2)

            def slot(k, turn):
                it, after, old = item(k, turn), item(k + 1, turn), item(k - 2, turn)
                if after is not None and after.layer == 0 and k > 0:
                    low_half_of_x(after)
                if old is not None:
                    wait_items(pool, square_done, old)
                    nc.gpsimd.tensor_tensor(var_eps[old.n2][:], square_sum[old.n2][:], d_eps[:],
                                            ALU.add).then_inc(var_done, 1)
                    wait_items(pool, var_done, old)
                    nc.gpsimd.tensor_tensor(rstd[old.n2][:], var_eps[old.n2][:], minus_half[:],
                                            ALU.pow).then_inc(rstd_done, 1)
                if it is not None:
                    if it.layer == 0:
                        pool.wait_ge(x_loaded[it.b4], it.round * DMA + DMA)
                    else:
                        pool.wait_ge(mid_done, it.b + 1)
                    wait_items(pool, y_done, it, lag=2)
                    src = x_in[it.b4] if it.layer == 0 else x_mid[it.b2]
                    nc.gpsimd.tensor_tensor(x_bias[it.n2][:], src[:], per_row(bo[it.layer]),
                                            ALU.add).then_inc(x_bias_done, 1)
                if old is not None and k - 2 < ITEMS - 1:
                    z = normal[old.n2]
                    wait_items(pool, rstd_done, old)
                    wait_items(pool, centred_done, old)
                    nc.gpsimd.tensor_tensor(z[:], centred[old.n2][:],
                                            rstd[old.n2][:].unsqueeze(2).to_broadcast([P, LC, D]),
                                            ALU.mult).then_inc(normal_done, 1)
                    wait_items(pool, normal_done, old)
                    if old.layer == 0:
                        if ORDER[k - 2][1] >= 2:
                            pool.wait_ge(xt_psum, old.b - 1)
                        nc.gpsimd.tensor_tensor(x_mid[old.b2][:], z[:], per_row(beta[0]), ALU.add).then_inc(mid_done, 1)
                    else:
                        if not isinstance(old.b, int) or old.b > 0:
                            pool.wait_ge(stored, old.b * DMA)
                        nc.gpsimd.tensor_tensor(x_out[:], z[:], per_row(beta[1]), ALU.add).then_inc(out_done, 1)
                if k == 1:
                    scale_gamma(1)

            run_slots(pool, slot)


_VECTORS = ("bo", "gamma", "beta")


def kernel(**inputs):
    import numpy as _np
    import concourse.bacc as _bacc
    from concourse import mybir as _mybir
    from concourse.bass_utils import run_bass_kernel_spmd as _run

    nc = _bacc.Bacc("TRN2", target_bir_lowering=False, num_devices=1)
    arrays = {}

    def dram_in(name, a):
        a = _np.ascontiguousarray(a)
        arrays[f"in_{name}_dram"] = a
        return nc.dram_tensor(f"in_{name}_dram", a.shape, _mybir.dt.from_np(a.dtype), kind="ExternalInput").ap()

    x, adj = dram_in("x", inputs["x"]), dram_in("adj", inputs["adj"])
    x_t = dram_in("x_t", _np.transpose(inputs["x"], (0, 2, 1)))
    weights = {}
    for l in range(LAYERS):
        for w in FACTORS:
            a = inputs[f"L{l}_gnn_{w[:2]}"]
            weights[l, w] = dram_in(f"L{l}_{w}", _np.transpose(a) if w.endswith("T") else a)
        for w in _VECTORS:
            weights[l, w] = dram_in(f"L{l}_{w}", inputs[f"L{l}_gnn_{w}"])
    out = nc.dram_tensor("out_dram", inputs["x"].shape, _mybir.dt.float32, kind="ExternalOutput").ap()
    gnn_two_layers(nc, x, x_t, adj, weights, out)
    r = _run(nc, [arrays], core_ids=[0])
    return r.results[0]["out_dram"]
```

```python
from contextlib import ExitStack

import concourse.bass as bass
from concourse import mybir

F32 = mybir.dt.float32
F32R = mybir.dt.float32r
BF16 = mybir.dt.bfloat16
I32 = mybir.dt.int32
ALU = mybir.AluOpType
ACT = mybir.ActivationFunctionType

P = 128
EPS = 1e-5
MASKED = 2.0 ** 127

LAYERS = 2
FACTORS = ("WqT", "WkT", "WvT", "Wo")
WARM_UP = 5
DMA = 16


class Item:

    def __init__(self, layer, n, b, n2, n4, b4, round, mask):
        self.layer, self.n, self.b = layer, n, b
        self.n2, self.n4, self.b4, self.round = n2, n4, b4, round
        self.mask = mask


def item_order(graphs):
    order = [(0, b) for b in range(5)] + [(1, 0), (1, 1)]
    for b in range(5, graphs - 1):
        order += [(0, b), (1, b - 3)]
    return order[:-1] + [(0, graphs - 1)] + [(1, b) for b in range(graphs - 5, graphs)]


def gnn_two_layers(nc, x, x_t, adj, weights, out):
    B, L, D = x.shape
    LC, DC = L // P, D // P
    assert (LC, DC) == (2, 2)
    ORDER = item_order(B)
    ITEMS = len(ORDER)
    POS = {pair: k for k, pair in enumerate(ORDER)}
    FIRST, BODY = 9, 8
    TURNS = (ITEMS - FIRST - 9) // BODY
    assert all(ORDER[k + BODY * t] == (ORDER[k][0], ORDER[k][1] + BODY // 2 * t)
               for k in range(FIRST - 2, FIRST + BODY + 2) for t in range(TURNS))
    SPARE, SPARE_MASK = (0, B - 5), 4
    DRAIN = 2
    SCALE = -1.0 / float(D) ** 0.5
    ROOT_D = float(D) ** 0.5

    def item(k, turn):
        if not 0 <= k < ITEMS:
            return None
        layer, b = ORDER[k]
        return Item(layer, n=turn * BODY + k, b=turn * (BODY // 2) + b, n2=k % 2, n4=k % 4, b4=b % 4,
                    round=turn + b // 4, mask=SPARE_MASK if b in SPARE and isinstance(turn, int) else b % 4)

    def wait_items(eng, sem, it, lag=0):
        if isinstance(it.n, int) and it.n - lag + 1 <= 0:
            return
        eng.wait_ge(sem, it.n + (1 - lag))

    def run_slots(eng, slot):
        for k in range(FIRST):
            slot(k, 0)
        with eng.Fori(0, TURNS) as turn:
            for k in range(FIRST, FIRST + BODY):
                slot(k, turn)
        for k in range(FIRST + BODY * TURNS, ITEMS + DRAIN):
            slot(k, 0)

    with ExitStack() as ctx:
        def sb(name, shape, dt=F32):
            return ctx.enter_context(nc.sbuf_tensor(name, shape, dt))

        def bank(name):
            return ctx.enter_context(nc.psum_tensor(name, [P, 2, 256], F32))

        def sem(name):
            return ctx.enter_context(nc.semaphore(name))

        ident = sb("ident", [P, P])
        minus_half = sb("minus_half", [P, LC])
        d_eps = sb("d_eps", [P, LC])
        a_hi = [sb(f"a_hi{l}", [P, DC, D], F32R) for l in range(LAYERS)]
        a_lo = [sb(f"a_lo{l}", [P, DC, D], F32R) for l in range(LAYERS)]
        hc_hi = [[sb(f"hc_hi{l}{i}", [P, DC, 2, L], F32R) for i in range(2)] for l in range(LAYERS)]
        hc_lo = [[sb(f"hc_lo{l}{i}", [P, DC, 2, L], F32R) for i in range(2)] for l in range(LAYERS)]
        bo = [sb(f"bo{l}", [P, D]) for l in range(LAYERS)]
        gamma = [sb(f"gamma{l}", [P, D]) for l in range(LAYERS)]
        beta = [sb(f"beta{l}", [P, D]) for l in range(LAYERS)]
        w_in = {(l, w): sb(f"w_{w}{l}", [P, DC, D]) for l in range(LAYERS) for w in FACTORS}
        xt_in = [sb(f"xt_in{i}", [P, DC, L]) for i in range(4)]
        x_in = [sb(f"x_in{i}", [P, LC, D]) for i in range(4)]
        adj_in = [sb(f"adj_in{i}", [P, LC, L], I32) for i in range(4)]
        mask = [sb(f"mask{i}", [P, LC, L], BF16) for i in range(5)]
        x_mid = [sb(f"x_mid{i}", [P, LC, D]) for i in range(4)]
        x_out = sb("x_out", [P, LC, D])
        xt_hi = [sb(f"xt_hi{i}", [P, DC, L], F32R) for i in range(4)]
        xt_lo = [sb(f"xt_lo{i}", [P, DC, L], F32R) for i in range(4)]
        v_hi = [sb(f"v_hi{i}", [P, LC, D], F32R) for i in range(2)]
        v_lo = [sb(f"v_lo{i}", [P, LC, D], F32R) for i in range(2)]
        prob = sb("prob", [P, LC, L])
        pt_hi = sb("pt_hi", [P, LC, L], F32R)
        pt_lo = sb("pt_lo", [P, LC, L], F32R)
        x_bias = [sb(f"x_bias{i}", [P, LC, D]) for i in range(2)]
        y = [sb(f"y{i}", [P, LC, D]) for i in range(2)]
        centred = [sb(f"centred{i}", [P, LC, D]) for i in range(2)]
        normal = [sb(f"normal{i}", [P, LC, D]) for i in range(2)]
        square = [sb(f"square{i}", [P, LC, D]) for i in range(2)]
        neg_max = [sb(f"neg_max{i}", [P, LC]) for i in range(2)]
        row_sum = [sb(f"row_sum{i}", [P, LC]) for i in range(2)]
        row_inv = [sb(f"row_inv{i}", [P, LC]) for i in range(2)]
        y_sum = [sb(f"y_sum{i}", [P, LC]) for i in range(2)]
        neg_mean = [sb(f"neg_mean{i}", [P, LC]) for i in range(2)]
        square_sum = [sb(f"square_sum{i}", [P, LC]) for i in range(2)]
        var_eps = [sb(f"var_eps{i}", [P, LC]) for i in range(2)]
        rstd = [sb(f"rstd{i}", [P, LC]) for i in range(2)]

        ps_xt, ps_h, ps_pt, ps_o = (bank(n) for n in ("ps_xt", "ps_h", "ps_pt", "ps_o"))
        ps_sv = [ctx.enter_context(nc.psum_tensor(f"ps_sv{i}", [P, LC, 2, L], F32)) for i in range(2)]
        ps_w = [[ps_sv[1][:, 0], ps_sv[1][:, 1]], [ps_xt[:], ps_sv[0][:, 0]]]

        last_out = normal[(ITEMS - 1) % 2]

        qk_loaded = [sem(f"qk_loaded{l}") for l in range(LAYERS)]
        vo_loaded = [sem(f"vo_loaded{l}") for l in range(LAYERS)]
        vec_loaded = [sem(f"vec_loaded{l}") for l in range(LAYERS)]
        xt_loaded = [sem(f"xt_loaded{i}") for i in range(4)]
        x_loaded = [sem(f"x_loaded{i}") for i in range(4)]
        adj_loaded = [sem(f"adj_loaded{i}") for i in range(4)]
        stored = sem("stored")
        ident_zero, ident_done, consts_done, gamma_done = (
            sem(n) for n in ("ident_zero", "ident_done", "consts_done", "gamma_done"))
        w_psum, w_hi_done, w_lo_done = (sem(n) for n in ("w_psum", "w_hi_done", "w_lo_done"))
        h_psum, pt_psum, o_psum = (sem(n) for n in ("h_psum", "pt_psum", "o_psum"))
        sv_psum = [sem(f"sv_psum{c}") for c in range(LC)]
        s_masked = [sem(f"s_masked{c}") for c in range(LC)]
        xt_hi_done, h_hi_done, v_hi_done, pt_hi_done = (
            sem(n) for n in ("xt_hi_done", "h_hi_done", "v_hi_done", "pt_hi_done"))
        xt_lo_done, h_lo_done, v_lo_done, pt_lo_done = (
            sem(n) for n in ("xt_lo_done", "h_lo_done", "v_lo_done", "pt_lo_done"))
        prob_done, inv_done, y_done, mean_done, square_done = (
            sem(n) for n in ("prob_done", "inv_done", "y_done", "mean_done", "square_done"))
        x_bias_done, centred_done, var_done, rstd_done, normal_done = (
            sem(n) for n in ("x_bias_done", "centred_done", "var_done", "rstd_done", "normal_done"))
        mask_done, xt_psum, mid_done, out_done = (sem(n) for n in ("mask_done", "xt_psum", "mid_done", "out_done"))
        last_done = sem("last_done")

        x_rows = x.rearrange("b (c p) d -> b p c d", p=P)
        xt_rows = x_t.rearrange("b (c p) l -> b p c l", p=P)
        adj_rows = adj.rearrange("b (c p) m -> b p c m", p=P)
        out_rows = out.rearrange("b (c p) d -> b p c d", p=P)

        def h_bank(k):
            return ps_xt if k == 1 else ps_h

        def o_bank(k):
            return ps_h if k == ITEMS - 1 else ps_o

        block = ctx.enter_context(nc.Block())

        @block.sync
        def _(sp):
            def load(dst, src, loaded):
                sp.dma_start(dst[:], src).then_inc(loaded, DMA)

            def load_weight(l, w, loaded):
                load(w_in[l, w], weights[l, w].rearrange("(c p) n -> p c n", p=P), loaded[l])

            def load_xt(b):
                load(xt_in[b], xt_rows[b], xt_loaded[b])

            def load_adj(b):
                load(adj_in[b], adj_rows[b], adj_loaded[b])

            def load_x(b):
                load(x_in[b], x_rows[b], x_loaded[b])

            def load_vectors(l):
                for tile, name in ((bo, "bo"), (gamma, "gamma"), (beta, "beta")):
                    load(tile[l], weights[l, name].partition_broadcast(P), vec_loaded[l])

            load_weight(0, "WqT", qk_loaded)
            load_weight(0, "WkT", qk_loaded)
            load_xt(0)
            load_weight(0, "WvT", vo_loaded)
            load_weight(0, "Wo", vo_loaded)
            load_xt(1)
            load_adj(0)
            load_xt(2)
            load_x(0)
            load_weight(1, "WqT", qk_loaded)
            load_weight(1, "WkT", qk_loaded)
            load_vectors(0)
            load_adj(1)
            load_xt(3)
            load_x(1)
            load_adj(2)
            load_weight(1, "WvT", vo_loaded)
            load_weight(1, "Wo", vo_loaded)
            load_x(2)
            load_adj(3)
            load_x(3)
            load_vectors(1)

            def slot(k, turn):
                old = item(k - 2, turn)
                if old is not None and old.layer == 0 and ORDER[k - 2][1] + 4 < B:
                    wait_items(sp, xt_lo_done, old)
                    load(xt_in[old.b4], xt_rows[old.b + 4], xt_loaded[old.b4])
                    wait_items(sp, x_bias_done, old)
                    load(x_in[old.b4], x_rows[old.b + 4], x_loaded[old.b4])
                    sp.wait_ge(mask_done, old.b + 1)
                    load(adj_in[old.b4], adj_rows[old.b + 4], adj_loaded[old.b4])
                if old is not None and old.layer == 1 and k - 2 < ITEMS - 2:
                    sp.wait_ge(out_done, old.b + 1)
                    sp.dma_start(out_rows[old.b], x_out[:]).then_inc(stored, DMA)

            run_slots(sp, slot)
            for i, (b, tile) in enumerate(((B - 2, x_out), (B - 1, last_out))):
                for c in range(LC):
                    sp.wait_ge(last_done, i * LC + c + 1)
                    sp.dma_start(out_rows[b][:, c, :], tile[:, c, :]).then_inc(stored, DMA)
            sp.wait_ge(stored, DMA * (B - 2 + 2 * LC))

        @block.tensor
        def _(pe):
            def transpose4(dst, src):
                for f in range(2):
                    for r in range(2):
                        last = nc.tensor.transpose(dst[:, f, r * P:(r + 1) * P], src[:, r, f * P:(f + 1) * P],
                                                   ident[:])
                return last

            def product(dst, lhs_hi, lhs_lo, rhs_hi, rhs_lo):
                for r in range(2):
                    rows = slice(r * P, (r + 1) * P)
                    terms = [(h, g, f) for f in range(2)
                             for h, g in ((lhs_lo, rhs_hi), (lhs_hi, rhs_lo), (lhs_hi, rhs_hi))]
                    for i, (h, g, f) in enumerate(terms):
                        last = nc.tensor.matmul(dst[:, r, :], h[:, f, rows], g[:, f, :],
                                                start=(i == 0), stop=(i == len(terms) - 1))
                return last

            def combine_weights(l, i):
                lhs, rhs, loaded = ("WkT", "WqT", qk_loaded) if i == 0 else ("WvT", "Wo", vo_loaded)
                pe.wait_ge(loaded[l], 2 * DMA)
                if (l, i) == (1, 0):
                    pe.wait_ge(h_lo_done, 2)
                if (l, i) == (1, 1):
                    pe.wait_ge(v_lo_done, 3)
                for r in range(2):
                    for f in range(2):
                        last = nc.tensor.matmul(ps_w[l][i][:, r, :], w_in[l, lhs][:, f, r * P:(r + 1) * P],
                                                w_in[l, rhs][:, f, :], start=(f == 0), stop=(f == 1))
                last.then_inc(w_psum, 1)

            pe.wait_ge(ident_done, 1)
            for i in range(WARM_UP):
                nc.tensor.matmul(ps_xt[:, 0, 0:P], ident[:], ident[:], start=True, stop=True)
            combine_weights(0, 0)
            combine_weights(0, 1)

            def project(it, k):
                if k == 0 or k == POS[1, 0]:
                    pe.wait_ge(w_lo_done, 1 if k == 0 else 4)
                wait_items(pe, xt_lo_done, it)
                wait_items(pe, h_lo_done, it, lag=2 if k in (1, 2) else 1)
                product(h_bank(k), a_hi[it.layer], a_lo[it.layer], xt_hi[it.n4], xt_lo[it.n4]).then_inc(h_psum, 1)

            def scores_and_values(it, k):
                if k == 0:
                    pe.wait_ge(w_lo_done, 2)
                elif k == 1:
                    pe.wait_ge(w_lo_done, 3)
                elif k == 4:
                    pe.wait_ge(w_lo_done, 6)
                wait_items(pe, h_lo_done, it)
                wait_items(pe, v_lo_done, it, lag=2)
                xh, xl, hh, hl = xt_hi[it.n4], xt_lo[it.n4], hc_hi[it.layer][it.n2], hc_lo[it.layer][it.n2]
                for c in range(LC):
                    rows = slice(c * P, (c + 1) * P)
                    terms = [(u, w, f) for f in range(DC) for u, w in ((xl, hh), (xh, hl), (xh, hh))]
                    for i, (u, w, f) in enumerate(terms):
                        last = nc.tensor.matmul(ps_sv[it.n2][:, c, :, :], u[:, f, rows], w[:, f, :, :],
                                                start=(i == 0), stop=(i == len(terms) - 1))
                    last.then_inc(sv_psum[c], 1)

            def slot(k, turn):
                it, before, after, later = (item(k + d, turn) for d in (0, -1, 1, 2))
                if after is not None:
                    project(after, k + 1)
                if k == 1:
                    combine_weights(1, 0)
                if before is not None:
                    wait_items(pe, prob_done, before)
                    transpose4(ps_pt, prob).then_inc(pt_psum, 1)
                if k == 3:
                    combine_weights(1, 1)
                if later is not None and later.layer == 1:
                    if k + 2 == POS[1, 0]:
                        pe.wait_ge(w_lo_done, 4)
                    pe.wait_ge(mid_done, later.b + 1)
                    transpose4(ps_xt, x_mid[later.b4]).then_inc(xt_psum, 1)
                if it is not None:
                    scores_and_values(it, k)
                if before is not None:
                    wait_items(pe, pt_lo_done, before)
                    wait_items(pe, v_lo_done, before)
                    wait_items(pe, y_done, before, lag=2 if k == ITEMS else 1)
                    product(o_bank(k - 1), pt_hi, pt_lo, v_hi[before.n2], v_lo[before.n2]).then_inc(o_psum, 1)

            project(item(0, 0), 0)
            run_slots(pe, slot)

        @block.scalar
        def _(act):
            def split_a(l):
                act.wait_ge(w_psum, 2 * l + 1)
                nc.scalar.activation(a_hi[l][:], ps_w[l][0], ACT.Copy, scale=SCALE).then_inc(w_hi_done, 1)

            def split_c(l):
                act.wait_ge(w_psum, 2 * l + 2)
                nc.scalar.activation(hc_hi[l][0][:, :, 1, :], ps_w[l][1], ACT.Copy).then_inc(w_hi_done, 1)

            def copy_c(l):
                act.wait_ge(w_hi_done, 3 * l + 2)
                nc.scalar.activation(hc_hi[l][1][:, :, 1, :], hc_hi[l][0][:, :, 1, :].bitcast(F32),
                                     ACT.Copy).then_inc(w_hi_done, 1)

            def high_half(it, psum_ready, dst, src, done):
                wait_items(act, psum_ready, it)
                nc.scalar.activation(dst, src, ACT.Copy).then_inc(done, 1)

            def high_half_of_x(it):
                wait_items(act, sv_psum[1], it, lag=4)
                if it.layer == 1:
                    act.wait_ge(xt_psum, it.b + 1)
                    src = ps_xt
                else:
                    act.wait_ge(xt_loaded[it.b4], it.round * DMA + DMA)
                    src = xt_in[it.b4]
                nc.scalar.activation(xt_hi[it.n4][:], src[:], ACT.Copy).then_inc(xt_hi_done, 1)

            def high_half_of_h(it, k):
                high_half(it, h_psum, hc_hi[it.layer][it.n2][:, :, 0, :], h_bank(k)[:], h_hi_done)

            def slot(k, turn):
                it, before, after, later, old = (item(k + d, turn) for d in (0, -1, 1, 2, -2))
                if later is not None and later.layer == 0:
                    high_half_of_x(later)
                if after is not None:
                    high_half_of_h(after, k + 1)
                if k == 0:
                    copy_c(0)
                if before is not None:
                    high_half(before, pt_psum, pt_hi[:], ps_pt[:], pt_hi_done)
                if old is not None:
                    wait_items(act, mean_done, old)
                    for c in range(LC):
                        last = nc.scalar.activation(square[old.n2][:, c, :], y[old.n2][:, c, :], ACT.Square,
                                                    bias=neg_mean[old.n2][:, c:c + 1],
                                                    accum_out=square_sum[old.n2][:, c:c + 1])
                    last.then_inc(square_done, 1)
                if later is not None and later.layer == 1:
                    high_half_of_x(later)
                if k == 2:
                    split_a(1)
                if k == 3:
                    split_c(1)
                    copy_c(1)
                if it is not None:
                    for c in range(LC):
                        wait_items(act, s_masked[c], it)
                        last = nc.scalar.activation(prob[:, c, :], ps_sv[it.n2][:, c, 0, :], ACT.Exp, scale=-1.0,
                                                    bias=neg_max[it.n2][:, c:c + 1],
                                                    accum_out=row_sum[it.n2][:, c:c + 1])
                        if c == LC - 1:
                            last.then_inc(prob_done, 1)
                        last = nc.scalar.activation(v_hi[it.n2][:, c, :], ps_sv[it.n2][:, c, 1, :], ACT.Copy)
                    last.then_inc(v_hi_done, 1)

            high_half_of_x(item(0, 0))
            high_half_of_x(item(1, 0))
            split_a(0)
            split_c(0)
            high_half_of_h(item(0, 0), 0)
            run_slots(act, slot)

        @block.vector
        def _(dve):
            nc.vector.memset(minus_half[:], -0.5).then_inc(consts_done, 1)
            nc.vector.memset(d_eps[:], D * EPS).then_inc(consts_done, 1)

            def split_a(l):
                dve.wait_ge(w_hi_done, 3 * l + 1)
                nc.vector.scalar_tensor_tensor(a_lo[l][:], ps_w[l][0], SCALE, a_hi[l][:].bitcast(F32),
                                               ALU.mult, ALU.subtract).then_inc(w_lo_done, 1)

            def split_c(l):
                dve.wait_ge(w_hi_done, 3 * l + 2)
                nc.vector.tensor_tensor(hc_lo[l][0][:, :, 1, :], ps_w[l][1],
                                        hc_hi[l][0][:, :, 1, :].bitcast(F32), ALU.subtract).then_inc(w_lo_done, 1)

            def copy_c(l):
                dve.wait_ge(w_lo_done, 3 * l + 2)
                dve.wait_ge(w_hi_done, 3 * l + 3)
                nc.vector.tensor_copy(hc_lo[l][1][:, :, 1, :],
                                      hc_lo[l][0][:, :, 1, :].bitcast(F32)).then_inc(w_lo_done, 1)

            def low_half(it, hi_done, dst, src, hi, done):
                wait_items(dve, hi_done, it)
                nc.vector.tensor_tensor(dst, src, hi.bitcast(F32), ALU.subtract).then_inc(done, 1)

            def low_half_of_h(it, k):
                low_half(it, h_hi_done, hc_lo[it.layer][it.n2][:, :, 0, :], h_bank(k)[:],
                         hc_hi[it.layer][it.n2][:, :, 0, :], h_lo_done)

            def low_half_of_pt(it):
                low_half(it, pt_hi_done, pt_lo[:], ps_pt[:], pt_hi[:], pt_lo_done)

            def urgent(k):
                return k < ITEMS and ORDER[k][0] == 0 and POS[1, ORDER[k][1]] - k == 5

            def centre(it, k):
                wait_items(dve, normal_done, it, lag=2)
                if k in (0, POS[1, 0]):
                    dve.wait_ge(gamma_done, ORDER[k][0] + 1)
                wait_items(dve, mean_done, it)
                for c in range(LC):
                    last = nc.vector.scalar_tensor_tensor(centred[it.n2][:, c, :], y[it.n2][:, c, :],
                                                          neg_mean[it.n2][:, c:c + 1], gamma[it.layer][:],
                                                          ALU.add, ALU.mult)
                last.then_inc(centred_done, 1)

            def finish(it, dst, free):
                wait_items(dve, rstd_done, it)
                wait_items(dve, centred_done, it)
                dve.wait_ge(*free)
                for c in range(LC):
                    nc.vector.scalar_tensor_tensor(dst[:, c, :], centred[it.n2][:, c, :], rstd[it.n2][:, c:c + 1],
                                                   beta[1][:], ALU.mult, ALU.add).then_inc(last_done, 1)

            def mask_scores(it, before, c):
                if it is not None:
                    wait_items(dve, sv_psum[c], it)
                    dve.wait_ge(mask_done, it.b + 1)
                if before is not None:
                    last = nc.vector.reciprocal(row_inv[before.n2][:, c:c + 1], row_sum[before.n2][:, c:c + 1])
                    if c == LC - 1:
                        last.then_inc(inv_done, 1)
                if it is not None:
                    nc.vector.tensor_tensor_reduce(out=ps_sv[it.n2][:, c, 0, :], in0=ps_sv[it.n2][:, c, 0, :],
                                                   in1=mask[it.mask][:, c, :], scale=1.0, scalar=3.0e38,
                                                   op0=ALU.add, op1=ALU.min,
                                                   accum_out=neg_max[it.n2][:, c:c + 1]).then_inc(s_masked[c], 1)

            def slot(k, turn):
                it, before, after, later, old = (item(k + d, turn) for d in (0, -1, 1, 2, -2))
                if k == ITEMS:
                    low_half_of_pt(before)
                if old is not None:
                    wait_items(dve, square_done, old, lag=2)
                    wait_items(dve, inv_done, old)
                    wait_items(dve, o_psum, old)
                    wait_items(dve, x_bias_done, old)
                    for c in range(LC):
                        last = nc.vector.scalar_tensor_tensor(y[old.n2][:, c, :], o_bank(k - 2)[:, c, :],
                                                              row_inv[old.n2][:, c:c + 1], x_bias[old.n2][:, c, :],
                                                              ALU.mult, ALU.add, accum_out=y_sum[old.n2][:, c:c + 1])
                    last.then_inc(y_done, 1)
                    wait_items(dve, y_done, old)
                    nc.vector.tensor_scalar(neg_mean[old.n2][:], y_sum[old.n2][:], -1.0 / D, None,
                                            ALU.mult).then_inc(mean_done, 1)
                if after is not None:
                    low_half_of_h(after, k + 1)
                if k == 0:
                    copy_c(0)
                if before is not None and k < ITEMS:
                    low_half_of_pt(before)
                if old is not None and urgent(k - 2):
                    centre(old, k - 2)
                mask_scores(it, before, 0)
                if later is not None and later.layer == 1:
                    low_half(later, xt_hi_done, xt_lo[later.n4][:], ps_xt[:], xt_hi[later.n4][:], xt_lo_done)
                mask_scores(it, before, 1)
                if old is not None and not urgent(k - 2):
                    centre(old, k - 2)
                if k == ITEMS + 1:
                    finish(item(ITEMS - 2, 0), x_out, (stored, DMA * (B - 2)))
                    finish(old, last_out, (out_done, B - 2))
                if k == 2:
                    split_a(1)
                if k == 3:
                    split_c(1)
                    copy_c(1)
                if it is not None:
                    low_half(it, v_hi_done, v_lo[it.n2][:], ps_sv[it.n2][:, :, 1, :], v_hi[it.n2][:], v_lo_done)
                if after is not None and after.layer == 0:
                    make_mask(after)

            def make_mask(it):
                dve.wait_ge(adj_loaded[it.b4], it.round * DMA + DMA)
                nc.vector.tensor_scalar(mask[it.mask][:], adj_in[it.b4][:], 0.0, MASKED, ALU.is_equal,
                                        ALU.mult).then_inc(mask_done, 1)

            split_a(0)
            split_c(0)
            low_half_of_h(item(0, 0), 0)
            make_mask(item(0, 0))
            run_slots(dve, slot)

        @block.gpsimd
        def _(pool):
            nc.gpsimd.memset(ident[:], 0.0).then_inc(ident_zero, 1)
            pool.wait_ge(ident_zero, 1)
            nc.gpsimd.affine_select(out=ident[:], in_=ident[:], compare_op=ALU.not_equal, fill=1.0, base=0,
                                    pattern=[[-1, P]], channel_multiplier=1).then_inc(ident_done, 1)

            def scale_gamma(l):
                pool.wait_ge(vec_loaded[l], 3 * DMA)
                nc.gpsimd.tensor_scalar(gamma[l][:], gamma[l][:], ROOT_D, 0.0, ALU.mult,
                                        ALU.add).then_inc(gamma_done, 1)

            def per_row(tile):
                return tile[:].unsqueeze(1).to_broadcast([P, LC, D])

            def low_half_of_x(it):
                wait_items(pool, xt_hi_done, it)
                nc.gpsimd.tensor_tensor(xt_lo[it.n4][:], xt_in[it.b4][:], xt_hi[it.n4][:].bitcast(F32),
                                        ALU.subtract).then_inc(xt_lo_done, 1)

            low_half_of_x(item(0, 0))
            low_half_of_x(item(1, 0))
            scale_gamma(0)
            pool.wait_ge(consts_done, 2)

            def slot(k, turn):
                it, later, old = item(k, turn), item(k + 2, turn), item(k - 2, turn)
                if later is not None and later.layer == 0:
                    low_half_of_x(later)
                if old is not None:
                    wait_items(pool, square_done, old)
                    nc.gpsimd.tensor_tensor(var_eps[old.n2][:], square_sum[old.n2][:], d_eps[:],
                                            ALU.add).then_inc(var_done, 1)
                    wait_items(pool, var_done, old)
                    nc.gpsimd.tensor_tensor(rstd[old.n2][:], var_eps[old.n2][:], minus_half[:],
                                            ALU.pow).then_inc(rstd_done, 1)
                if old is not None and k - 2 < ITEMS - 2:
                    z = normal[old.n2]
                    wait_items(pool, rstd_done, old)
                    wait_items(pool, centred_done, old)
                    nc.gpsimd.tensor_tensor(z[:], centred[old.n2][:],
                                            rstd[old.n2][:].unsqueeze(2).to_broadcast([P, LC, D]),
                                            ALU.mult).then_inc(normal_done, 1)
                    wait_items(pool, normal_done, old)
                    if old.layer == 0:
                        if ORDER[k - 2][1] >= 4:
                            pool.wait_ge(xt_psum, old.b - 3)
                        nc.gpsimd.tensor_tensor(x_mid[old.b4][:], z[:], per_row(beta[0]), ALU.add).then_inc(mid_done, 1)
                    else:
                        if not isinstance(old.b, int) or old.b > 0:
                            pool.wait_ge(stored, old.b * DMA)
                        nc.gpsimd.tensor_tensor(x_out[:], z[:], per_row(beta[1]), ALU.add).then_inc(out_done, 1)
                if it is not None:
                    if it.layer == 0:
                        pool.wait_ge(x_loaded[it.b4], it.round * DMA + DMA)
                    else:
                        pool.wait_ge(mid_done, it.b + 1)
                    wait_items(pool, y_done, it, lag=2)
                    src = x_in[it.b4] if it.layer == 0 else x_mid[it.b4]
                    nc.gpsimd.tensor_tensor(x_bias[it.n2][:], src[:], per_row(bo[it.layer]),
                                            ALU.add).then_inc(x_bias_done, 1)
                if k == 1:
                    scale_gamma(1)

            run_slots(pool, slot)


_VECTORS = ("bo", "gamma", "beta")


def kernel(**inputs):
    import numpy as _np
    import concourse.bacc as _bacc
    from concourse import mybir as _mybir
    from concourse.bass_utils import run_bass_kernel_spmd as _run

    nc = _bacc.Bacc("TRN2", target_bir_lowering=False, num_devices=1)
    arrays = {}

    def dram_in(name, a):
        a = _np.ascontiguousarray(a)
        arrays[f"in_{name}_dram"] = a
        return nc.dram_tensor(f"in_{name}_dram", a.shape, _mybir.dt.from_np(a.dtype), kind="ExternalInput").ap()

    x, adj = dram_in("x", inputs["x"]), dram_in("adj", inputs["adj"])
    x_t = dram_in("x_t", _np.transpose(inputs["x"], (0, 2, 1)))
    weights = {}
    for l in range(LAYERS):
        for w in FACTORS:
            a = inputs[f"L{l}_gnn_{w[:2]}"]
            weights[l, w] = dram_in(f"L{l}_{w}", _np.transpose(a) if w.endswith("T") else a)
        for w in _VECTORS:
            weights[l, w] = dram_in(f"L{l}_{w}", inputs[f"L{l}_gnn_{w}"])
    out = nc.dram_tensor("out_dram", inputs["x"].shape, _mybir.dt.float32, kind="ExternalOutput").ap()
    gnn_two_layers(nc, x, x_t, adj, weights, out)
    r = _run(nc, [arrays], core_ids=[0])
    return r.results[0]["out_dram"]
```
